# Optimizing a Trainium2 kernel written in Bass

```python
import numpy as np
import jax
import jax.numpy as jnp

def _softmax(x, axis=-1):
    return jax.nn.softmax(x, axis=axis)

def _gelu(x):
    return jax.nn.gelu(x, approximate=True)

def _silu(x):
    return jax.nn.silu(x)

def _sigmoid(x):
    return jax.nn.sigmoid(x)

def _layernorm(x, axis=-1, eps=1e-05):
    m = jnp.mean(x, axis=axis, keepdims=True)
    v = jnp.var(x, axis=axis, keepdims=True)
    return (x - m) / jnp.sqrt(v + eps)

def _scatter_add(tgt, idx, src, axis=0):
    return tgt.at[idx].add(src)

def _segment_sum(src, seg, n):
    return jax.ops.segment_sum(src, seg, n)
kernel_name = 'mk_gnn_resnorm_d4_gnn_r16_421b92'

def setup_inputs(seed: int=0):
    np.random.seed(seed)
    _w = jnp.asarray

    def _rec_inputs():
        import jax
        import jax.numpy as jnp
        _gk = jax.random.key(seed)
        x = -0.0005121 + 1.001 * jax.random.normal(jax.random.fold_in(_gk, 1), (6250, 32), jnp.float32)
        _s = jax.random.randint(jax.random.fold_in(_gk, 2), (100000,), 0, 6250, jnp.int32)
        _d = jax.random.randint(jax.random.fold_in(_gk, 3), (100000,), 0, 6250, jnp.int32)
        _loop = jnp.arange(6250, dtype=jnp.int32)
        src = jnp.concatenate([_s, _d, _loop])
        dst = jnp.concatenate([_d, _s, _loop])
        _o = jnp.argsort(dst, stable=True)
        src = src[_o]
        dst = dst[_o]
        edge_attr_3 = jax.random.uniform(jax.random.fold_in(_gk, 12), (206250, 3), jnp.float32, 0.0, 1)
        edge_weight = jax.random.uniform(jax.random.fold_in(_gk, 14), (206250,), jnp.float32, 0.0, 1)
        return (x, src, dst, edge_attr_3, edge_weight)
    x, src, dst, edge_attr_3, edge_weight = _rec_inputs()

    def _L0_gnn_setup():
        import jax, jax.numpy as jnp
        import numpy as np
        N_NODES = 6250
        N_EDGES = 100000
        EMB_DIM = 32
        NUM_LAYERS = 3
        key = jax.random.key(seed)
        k_emb, k_w, k_row, k_col = jax.random.split(key, 4)
        emb = jax.random.normal(k_emb, (N_NODES, EMB_DIM), dtype=jnp.float32)
        edge_weight = jax.random.uniform(k_w, (N_EDGES,), dtype=jnp.float32)
        row = jax.random.randint(k_row, (N_EDGES,), 0, N_NODES, dtype=jnp.int32)
        col = jax.random.randint(k_col, (N_EDGES,), 0, N_NODES, dtype=jnp.int32)
        return {'emb': emb, 'edge_weight': edge_weight, 'row': row, 'col': col, 'num_layers': NUM_LAYERS}
    _L0_gnn_all = _L0_gnn_setup()
    _L0_gnn_in = {k: v for k, v in _L0_gnn_all.items() if k in ()}
    del _L0_gnn_all

    def _L1_gnn_setup():
        import jax, jax.numpy as jnp
        import numpy as np
        N = 3125
        E = 100000
        C = 32
        KS = 4
        DIM = 3
        K3 = KS ** DIM
        NEG = 0.01
        EPS = 1e-05
        _BITS = np.array([[s >> d & 1 for d in range(DIM)] for s in range(2 ** DIM)], dtype=np.int32)

        def _basis(edge_attr):
            v = edge_attr * (KS - 1)
            lo = jnp.floor(v)
            f = v - lo
            lo = lo.astype(jnp.int32)
            bits = jnp.asarray(_BITS)
            idx = jnp.clip(lo[:, None, :] + bits[None], 0, KS - 1)
            w = jnp.where(bits[None] == 1, f[:, None, :], 1.0 - f[:, None, :])
            basis = jnp.prod(w, axis=-1)
            wi = idx[..., 0] + KS * idx[..., 1] + KS * KS * idx[..., 2]
            return (basis, wi)

        def _sconv(x, src, dst, basis, wi, W, R, b):
            n = x.shape[0]
            z = jnp.einsum('nc,kco->nko', x, W)
            msg = jnp.zeros((src.shape[0], W.shape[2]), x.dtype)
            for s in range(basis.shape[1]):
                msg = msg + basis[:, s, None] * z[src, wi[:, s]]
            agg = jax.ops.segment_sum(msg, dst, num_segments=n)
            cnt = jax.ops.segment_sum(jnp.ones((dst.shape[0],), x.dtype), dst, num_segments=n)
            agg = agg / jnp.clip(cnt, 1.0)[:, None]
            return agg + x @ R + b

        def _bn(x, g, be):
            mu = x.mean(0)
            var = x.var(0)
            return (x - mu) * jax.lax.rsqrt(var + EPS) * g + be

        def _leaky(x):
            return jnp.where(x >= 0, x, NEG * x)
        key = jax.random.key(seed)
        ks = jax.random.split(key, 32)
        inp = {'patch_embs': jax.random.normal(ks[0], (N, C), jnp.float32), 'edge_index': jax.random.randint(ks[1], (2, E), 0, N, jnp.int32), 'edge_attr': jax.random.uniform(ks[2], (E, DIM), jnp.float32)}
        i = 3
        for l in (1, 2, 3):
            inp[f'W{l}'] = jax.random.normal(ks[i], (K3, C, C), jnp.float32) * 0.05
            i += 1
            inp[f'R{l}'] = jax.random.normal(ks[i], (C, C), jnp.float32) * 0.1
            i += 1
            inp[f'b{l}'] = jnp.zeros((C,), jnp.float32)
            inp[f'g{l}'] = jnp.ones((C,), jnp.float32)
            inp[f'be{l}'] = jnp.zeros((C,), jnp.float32)
        return inp
    _L1_gnn_all = _L1_gnn_setup()
    _L1_gnn_in = {k: v for k, v in _L1_gnn_all.items() if k in ('W1', 'R1', 'b1', 'g1', 'be1', 'W2', 'R2', 'b2', 'g2', 'be2', 'W3', 'R3', 'b3', 'g3', 'be3')}
    del _L1_gnn_all

    def _L2_gnn_setup():
        import jax, jax.numpy as jnp
        import numpy as np
        N_NODES = 6250
        N_EDGES = 100000
        N_FEAT = 32
        key = jax.random.key(seed)
        k1, k2, k3, k4 = jax.random.split(key, 4)
        u = jax.random.normal(k1, (N_NODES, N_FEAT), dtype=jnp.float32)
        weights = jax.random.uniform(k2, (N_EDGES,), dtype=jnp.float32)
        row = jax.random.randint(k3, (N_EDGES,), 0, N_NODES)
        col = jax.random.randint(k4, (N_EDGES,), 0, N_NODES)
        edge_index = jnp.stack([row, col]).astype(jnp.int64)
        return {'u': u, 'weights': weights, 'edge_index': edge_index}
    _L2_gnn_all = _L2_gnn_setup()
    _L2_gnn_in = {k: v for k, v in _L2_gnn_all.items() if k in ()}
    del _L2_gnn_all

    def _L3_gnn_setup():
        import jax, jax.numpy as jnp
        import numpy as np
        N_NODES = 6250
        N_EDGES = 100000
        D_FEAT = 32
        key = jax.random.key(seed)
        k1, k2 = jax.random.split(key)
        x = jax.random.normal(k1, (N_NODES, D_FEAT), dtype=jnp.float32)
        edge_neighbors = jax.random.randint(k2, (2, N_EDGES), 0, N_NODES, dtype=jnp.int64)
        return {'x': x, 'edge_neighbors': edge_neighbors}
    _L3_gnn_all = _L3_gnn_setup()
    _L3_gnn_in = {k: v for k, v in _L3_gnn_all.items() if k in ()}
    del _L3_gnn_all
    return {'x': x, 'src': src, 'dst': dst, 'edge_attr_3': edge_attr_3, 'edge_weight': edge_weight, 'L1_gnn_W1': _L1_gnn_in['W1'], 'L1_gnn_R1': _L1_gnn_in['R1'], 'L1_gnn_b1': _L1_gnn_in['b1'], 'L1_gnn_g1': _L1_gnn_in['g1'], 'L1_gnn_be1': _L1_gnn_in['be1'], 'L1_gnn_W2': _L1_gnn_in['W2'], 'L1_gnn_R2': _L1_gnn_in['R2'], 'L1_gnn_b2': _L1_gnn_in['b2'], 'L1_gnn_g2': _L1_gnn_in['g2'], 'L1_gnn_be2': _L1_gnn_in['be2'], 'L1_gnn_W3': _L1_gnn_in['W3'], 'L1_gnn_R3': _L1_gnn_in['R3'], 'L1_gnn_b3': _L1_gnn_in['b3'], 'L1_gnn_g3': _L1_gnn_in['g3'], 'L1_gnn_be3': _L1_gnn_in['be3']}

def reference(x, src, dst, edge_attr_3, edge_weight, L1_gnn_W1, L1_gnn_R1, L1_gnn_b1, L1_gnn_g1, L1_gnn_be1, L1_gnn_W2, L1_gnn_R2, L1_gnn_b2, L1_gnn_g2, L1_gnn_be2, L1_gnn_W3, L1_gnn_R3, L1_gnn_b3, L1_gnn_g3, L1_gnn_be3):
    import jax
    import jax.numpy as jnp

    def _L0_gnn_ref(emb, edge_weight, row, col, num_layers):
        import jax, jax.numpy as jnp
        import numpy as np
        N_NODES = 6250
        N_EDGES = 100000
        EMB_DIM = 32
        NUM_LAYERS = 3
        n = emb.shape[0]
        w = edge_weight[:, None]
        X = emb
        for _ in range(num_layers):
            msgs = w * X[col]
            X = jax.ops.segment_sum(msgs, row, num_segments=n)
        return X

    def _L1_gnn_ref(patch_embs, edge_index, edge_attr, W1, R1, b1, g1, be1, W2, R2, b2, g2, be2, W3, R3, b3, g3, be3):
        import jax, jax.numpy as jnp
        import numpy as np
        N = 3125
        E = 100000
        C = 32
        KS = 4
        DIM = 3
        K3 = KS ** DIM
        NEG = 0.01
        EPS = 1e-05
        _BITS = np.array([[s >> d & 1 for d in range(DIM)] for s in range(2 ** DIM)], dtype=np.int32)

        def _basis(edge_attr):
            v = edge_attr * (KS - 1)
            lo = jnp.floor(v)
            f = v - lo
            lo = lo.astype(jnp.int32)
            bits = jnp.asarray(_BITS)
            idx = jnp.clip(lo[:, None, :] + bits[None], 0, KS - 1)
            w = jnp.where(bits[None] == 1, f[:, None, :], 1.0 - f[:, None, :])
            basis = jnp.prod(w, axis=-1)
            wi = idx[..., 0] + KS * idx[..., 1] + KS * KS * idx[..., 2]
            return (basis, wi)

        def _sconv(x, src, dst, basis, wi, W, R, b):
            n = x.shape[0]
            z = jnp.einsum('nc,kco->nko', x, W)
            msg = jnp.zeros((src.shape[0], W.shape[2]), x.dtype)
            for s in range(basis.shape[1]):
                msg = msg + basis[:, s, None] * z[src, wi[:, s]]
            agg = jax.ops.segment_sum(msg, dst, num_segments=n)
            cnt = jax.ops.segment_sum(jnp.ones((dst.shape[0],), x.dtype), dst, num_segments=n)
            agg = agg / jnp.clip(cnt, 1.0)[:, None]
            return agg + x @ R + b

        def _bn(x, g, be):
            mu = x.mean(0)
            var = x.var(0)
            return (x - mu) * jax.lax.rsqrt(var + EPS) * g + be

        def _leaky(x):
            return jnp.where(x >= 0, x, NEG * x)
        src, dst = (edge_index[0], edge_index[1])
        basis, wi = _basis(edge_attr)
        x = _bn(_leaky(_sconv(patch_embs, src, dst, basis, wi, W1, R1, b1)) + patch_embs, g1, be1)
        x = _bn(_leaky(_sconv(x, src, dst, basis, wi, W2, R2, b2)) + x, g2, be2)
        x = _bn(_sconv(x, src, dst, basis, wi, W3, R3, b3) + x, g3, be3)
        return x

    def _L2_gnn_ref(u, weights, edge_index):
        import jax, jax.numpy as jnp
        import numpy as np
        N_NODES = 6250
        N_EDGES = 100000
        N_FEAT = 32
        row, col = (edge_index[0], edge_index[1])
        diff = u[col] - u[row]
        weighted_diff = weights[:, None] * diff
        laplacian = jax.ops.segment_sum(weighted_diff, row, num_segments=u.shape[0])
        return laplacian

    def _L3_gnn_ref(x, edge_neighbors):
        import jax, jax.numpy as jnp
        import numpy as np
        N_NODES = 6250
        N_EDGES = 100000
        D_FEAT = 32
        msgs = x[edge_neighbors[1]]
        out = jax.ops.segment_sum(msgs, edge_neighbors[0], num_segments=x.shape[0])
        return out
    edge_index = jnp.stack([src, dst])
    x = _layernorm(x + _L0_gnn_ref(x, edge_weight, src, dst, 3), axis=-1)
    x = _layernorm(x + _L1_gnn_ref(x, edge_index, edge_attr_3, L1_gnn_W1, L1_gnn_R1, L1_gnn_b1, L1_gnn_g1, L1_gnn_be1, L1_gnn_W2, L1_gnn_R2, L1_gnn_b2, L1_gnn_g2, L1_gnn_be2, L1_gnn_W3, L1_gnn_R3, L1_gnn_b3, L1_gnn_g3, L1_gnn_be3), axis=-1)
    x = _layernorm(x + _L2_gnn_ref(x, edge_weight, edge_index), axis=-1)
    x = _layernorm(x + _L3_gnn_ref(x, edge_index), axis=-1)
    return x

_drawn_inputs = setup_inputs


def setup_inputs(seed=0):
    import zlib

    import numpy as np

    out = dict(_drawn_inputs(seed))
    spreads = {'L1_gnn_b1': (0.0, 0.28),
     'L1_gnn_g1': (1.0, 0.2),
     'L1_gnn_be1': (0.0, 0.574),
     'L1_gnn_b2': (0.0, 0.288),
     'L1_gnn_g2': (1.0, 0.2),
     'L1_gnn_be2': (0.0, 0.8),
     'L1_gnn_b3': (0.0, 0.8),
     'L1_gnn_g3': (1.0, 0.2),
     'L1_gnn_be3': (0.0, 0.521)}
    factors = {'edge_attr_3': 3.53, 'L1_gnn_W1': 4.726, 'L1_gnn_W2': 5.967, 'L1_gnn_W3': 4.592}
    for name, (base, spread) in spreads.items():
        noise = np.random.default_rng([zlib.crc32(name.encode()), seed]).standard_normal(out[name].shape)
        drawn = base * np.exp(spread * noise) if base else spread * noise
        out[name] = jnp.asarray(drawn.astype(out[name].dtype))
    for name, factor in factors.items():
        out[name] = (out[name] * factor).astype(out[name].dtype)
    return out
```

```python
from contextlib import ExitStack, contextmanager

import concourse.bass as bass
from concourse import mybir

F32 = mybir.dt.float32
F16 = mybir.dt.float16
BF16 = mybir.dt.bfloat16
I32 = mybir.dt.int32
ALU = mybir.AluOpType
ACT = mybir.ActivationFunctionType
AX = mybir.AxisListType

P = 128
C = 32
NODES = 6250
M = 64
NP = -(-NODES // M)
NPAD = NP * M
EDGES = 206250
J = 8
GROUPS = 2 * -(-EDGES // (2 * J * P))
TILES = GROUPS * J
TPAD = TILES + 2 * J
WINDOW = 128
KS = 4
K3 = KS ** 3
ROW = (KS * KS + KS + 2) * C
Q = 4
POS = NPAD // Q
BANK = 512
QBANKS = 4
QCOLS = POS // QBANKS
RING = 4
EPS = 1e-05
NEG = 0.01
CHUNKS = 4
CT = TILES // CHUNKS


class Memory:

    def __init__(self, nc, ctx):
        def sb(name, shape, dt):
            return ctx.enter_context(nc.sbuf_tensor(name, shape, dt))

        self.src = sb("src_of_edge", [P, TPAD], I32)
        self.dst = sb("dst_of_edge", [P, TPAD], I32)
        self.zrow = sb("zrow_of_edge", [P, TPAD], I32)
        self.weight = sb("weight_of_edge", [P, TILES], F32)
        self.rel = sb("dst_in_window", [P, TILES], F32)
        self.base = sb("window_base", [1, GROUPS], I32)
        self.index = sb("index_slots", [P, 2, 2, J], I32)
        self.stage = sb("gathered", [P, 2, J, ROW], F32)
        self.prod = sb("corner_products", [P, J, 8, C], F32)
        self.spline = sb("spline_slots", [P, 2, J * 8], F32)
        self.msg = sb("messages", [P, 2, J, C], F32)
        self.onehot = sb("window_onehot", [P, 2, J, WINDOW], F32)
        self.acc = sb("sums", [P, NPAD + WINDOW], F32)
        self.part = sb("message_parts", [P, 3, J, C], BF16)
        self.rest = sb("message_rest", [P, 2, J, C], F32)
        self.qmask = sb("row_mask", [P, J, Q], BF16)
        self.qpos_i = sb("row_and_column_int", [P, 2, J], I32)
        self.qpos = sb("row_and_column", [P, 2, 2, J], F32)
        self.lhs = sb("spread_parts", [P, 2, J, 3, Q, C], BF16)
        self.wide = sb("all_node_onehot", [P, RING, POS], BF16)
        self.iota_pos = sb("iota_pos", [P, POS], F16)
        self.iota_win = sb("iota_window", [P, WINDOW], F32)
        self.ident = sb("identity", [P, P], F32)
        self.ones = sb("ones", [P, P], F32)
        self.small_row = sb("window_base_row", [1, GROUPS], F32)[:, :]
        self.zeros = sb("zeros", [P, BANK], BF16)
        self.x = sb("x_nm", [NP, M * C], F32)
        self.y = sb("y_nm", [NP, M * C], F32)
        self.h = sb("h_nm", [NP, M * C], F32)
        self.t = sb("t_nm", [NP, M * C], F32)
        self.stat = sb("stat_nm", [NP, 3, M], F32)
        self.inv_count = sb("inverse_count", [NP, M], F32)
        self.mask = sb("real_node", [NP, M], F32)
        self.vec = sb("vectors", [NP, 8, C], F32)
        self.root = sb("root_matrix", [C, C], F32)
        self.xslot = sb("x_columns", [NP, 2, C], F32)
        self.xtslot = sb("x_transposed", [C, 2, NP], F32)
        self.flag = sb("unsorted_flag", [1, 1], I32)
        self.small = sb("small", [P, 8], F32)
        self.ps = ctx.enter_context(nc.psum_tensor("ps", [P, 8, BANK], F32))

        flat_stage = self.stage[:, :, :, :].rearrange("p a j r -> p (a j r)")
        self.kernel_matrix = flat_stage[0:C, 0:K3 * C]
        self.zout = self.acc[0:NP, 0:2 * K3 * C].rearrange("p (a f) -> p a f", a=2)
        self.tmp = flat_stage[:, 0:27 * CT].rearrange("p (a t) -> p a t", t=CT)
        self.chunk_basis = self.acc[:, 0:CT * 8].rearrange("p (t k) -> p t k", k=8)

        self.table = nc.dram_tensor("node_table", [NPAD, C], F32).ap()
        self.z = nc.dram_tensor("z_table", [NPAD * K3, C], F32).ap()
        self.basis = nc.dram_tensor("basis_table", [P, TILES * 8], F32).ap()


class Chain:

    def __init__(self, eng, sem):
        self.eng, self.sem, self.n = eng, sem, 0

    def __call__(self, ins):
        self.n += 1
        ins.then_inc(self.sem, 1)
        self.eng.wait_ge(self.sem, self.n)


def pass_through(block, engines, sem):
    for name in engines.split():
        @{"sync": block.sync, "scalar": block.scalar, "gpsimd": block.gpsimd, "vector": block.vector}[name]
        def _(eng):
            eng.sem_inc(sem, 1)


@contextmanager
def semaphores(nc, phase, names):
    with ExitStack() as ctx:
        s = {n: ctx.enter_context(nc.semaphore(f"{phase}_{n}")) for n in names.split()}
        numbers = sorted(x.num for x in s.values())
        yield s
        while numbers:
            n = 1
            while n < len(numbers) and numbers[n] == numbers[0] + n:
                n += 1
            nc.sync.sem_clear(range(numbers[0], numbers[0] + n))
            numbers = numbers[n:]
        nc.all_engine_barrier()


def bcast(ap, n):
    return ap.unsqueeze(2).to_broadcast([ap.shape[0], ap.shape[1], n])


def setup(nc, ctx, mem, inp):
    with semaphores(nc, "setup", "loaded attr_loaded pool chain base_row base_all stored tmp_free max_t max_col") as s:
        a = mem.tmp

        with nc.Block() as block:
            @block.sync
            def _(sp):
                sp.dma_start(mem.src[:, :], inp["src"]).then_inc(s["loaded"], 16)
                sp.dma_start(mem.dst[:, :], inp["dst"]).then_inc(s["loaded"], 16)
                sp.dma_start(mem.weight[:, :], inp["edge_weight"]).then_inc(s["loaded"], 16)
                sp.dma_start(mem.x[:, :], inp["x"].rearrange("(p m) c -> p (m c)", m=M)).then_inc(s["loaded"], 16)
                for c in range(CHUNKS):
                    if c:
                        sp.wait_ge(s["tmp_free"], c)
                    sp.dma_start(a[:, 0:3, :], inp["edge_attr_3"][:, :, c * CT:(c + 1) * CT]).then_inc(s["attr_loaded"], 16)
                    sp.wait_ge(s["tmp_free"], c + 1)
                    sp.dma_start(mem.basis[:, c * CT * 8:(c + 1) * CT * 8],
                                 mem.chunk_basis.rearrange("p t k -> p (t k)")).then_inc(s["stored"], 16)
                sp.wait_ge(s["stored"], 16 * CHUNKS)

            @block.gpsimd
            def _(pool):
                nc.gpsimd.iota(mem.iota_pos[:, :], pattern=[[1, POS]], base=0, channel_multiplier=0,
                               allow_small_or_imprecise_dtypes=True).then_inc(s["pool"], 1)
                nc.gpsimd.iota(mem.iota_win[:, :], pattern=[[1, WINDOW]], base=0, channel_multiplier=0,
                               allow_small_or_imprecise_dtypes=True).then_inc(s["pool"], 1)
                nc.gpsimd.memset(mem.ones[:, :], 1.0).then_inc(s["pool"], 1)
                nc.gpsimd.memset(mem.zeros[:, :], 0.0).then_inc(s["pool"], 1)
                nc.gpsimd.memset(mem.ident[:, :], 0.0).then_inc(s["pool"], 1)
                nc.gpsimd.memset(mem.mask[:, :], 1.0).then_inc(s["pool"], 1)
                pool.wait_ge(s["pool"], 6)
                nc.gpsimd.affine_select(out=mem.ident[:, :], in_=mem.ident[:, :], compare_op=ALU.not_equal, fill=1.0,
                                        base=0, pattern=[[-1, P]], channel_multiplier=1).then_inc(s["pool"], 1)
                nc.gpsimd.affine_select(out=mem.mask[:, :], in_=mem.mask[:, :], compare_op=ALU.is_ge, fill=0.0,
                                        base=NODES - 1, pattern=[[-1, M]], channel_multiplier=-M).then_inc(s["pool"], 1)

            @block.tensor
            def _(pe):
                pe.wait_ge(s["pool"], 8)
                pe.wait_ge(s["base_row"], 1)
                nc.tensor.matmul(mem.ps[:, 0, 0:GROUPS], mem.ones[0:1, :], mem.small_row,
                                 start=True, stop=True).then_inc(s["base_all"], 1)
                pe.wait_ge(s["max_col"], 1)
                nc.tensor.matmul(mem.ps[0:1, 1, 0:P], mem.small[:, 2:3], mem.ident[:, :],
                                 start=True, stop=True).then_inc(s["max_t"], 1)

            @block.vector
            def _(dve):
                step = Chain(dve, s["chain"])
                v = nc.vector
                dve.wait_ge(s["loaded"], 64)
                step(v.tensor_copy(mem.rel[:, :], mem.dst[:, 0:TILES]))
                first = mem.rel[0:1, :].rearrange("p (g j) -> p g j", j=J)[:, :, 0]
                step(v.tensor_copy(mem.base[:, :], first))
                v.tensor_copy(mem.small_row, first).then_inc(s["base_row"], 1)
                dve.wait_ge(s["base_all"], 1)
                rel3 = mem.rel[:, :].rearrange("p (g j) -> p g j", j=J)
                step(v.tensor_tensor(rel3, rel3, bcast(mem.ps[:, 0, 0:GROUPS], J), ALU.subtract))
                step(v.tensor_reduce(mem.small[:, 0:1], mem.rel[:, :], AX.X, ALU.max))
                step(v.tensor_reduce(mem.small[:, 1:2], mem.rel[:, :], AX.X, ALU.min))
                step(v.tensor_scalar(mem.small[:, 0:1], mem.small[:, 0:1], -float(WINDOW - 1), None, ALU.add))
                step(v.tensor_scalar(mem.small[:, 1:2], mem.small[:, 1:2], -1.0, None, ALU.mult))
                v.tensor_tensor(mem.small[:, 2:3], mem.small[:, 0:1], mem.small[:, 1:2], ALU.max).then_inc(s["max_col"], 1)
                dve.wait_ge(s["max_t"], 1)
                step(v.tensor_reduce(mem.small[0:1, 3:4], mem.ps[0:1, 1, 0:P], AX.X, ALU.max))
                step(v.tensor_scalar(mem.flag[:, :], mem.small[0:1, 3:4], 0.0, None, ALU.is_gt))
                step(v.memset(mem.zrow[:, TILES:TPAD], 0))

                for c in range(CHUNKS):
                    dve.wait_ge(s["attr_loaded"], 16 * (c + 1))
                    if c:
                        dve.wait_ge(s["stored"], 16 * c)
                    for d in range(3):
                        val, low, cast, hi, ng, w0, w1, sel = (a[:, 3 + i, :] for i in range(8))
                        a0, a1, first_i = (a[:, 11 + 3 * d + i, :] for i in range(3))
                        step(v.tensor_scalar(val, a[:, d, :], float(KS - 1), -8.0, ALU.mult, ALU.max))
                        step(v.tensor_scalar(val, val, float(2 ** 20), None, ALU.min))
                        step(v.tensor_copy(cast.bitcast(I32), val))
                        step(v.tensor_copy(low, cast.bitcast(I32)))
                        step(v.tensor_tensor(hi, low, val, ALU.is_gt))
                        step(v.tensor_tensor(low, low, hi, ALU.subtract))
                        step(v.tensor_tensor(w1, val, low, ALU.subtract))
                        step(v.tensor_scalar(w0, w1, -1.0, 1.0, ALU.mult, ALU.add))
                        step(v.tensor_scalar(hi, low, float(KS - 1), None, ALU.is_ge))
                        step(v.tensor_scalar(ng, low, 0.0, None, ALU.is_lt))
                        step(v.tensor_scalar(first_i, low, 0.0, float(KS - 2), ALU.max, ALU.min))
                        step(v.tensor_tensor(sel, w0, hi, ALU.mult))
                        step(v.tensor_tensor(a0, w0, sel, ALU.subtract))
                        step(v.tensor_tensor(val, w1, ng, ALU.mult))
                        step(v.tensor_tensor(a1, w1, val, ALU.subtract))
                        step(v.tensor_tensor(a0, a0, val, ALU.add))
                        step(v.tensor_tensor(a1, a1, sel, ALU.add))
                    sl = slice(c * CT, (c + 1) * CT)
                    k = a[:, 3, :]
                    step(v.scalar_tensor_tensor(out=k, in0=a[:, 19, :], scalar=float(KS), in1=a[:, 16, :],
                                                op0=ALU.mult, op1=ALU.add))
                    step(v.scalar_tensor_tensor(out=k, in0=k, scalar=float(KS), in1=a[:, 13, :],
                                                op0=ALU.mult, op1=ALU.add))
                    step(v.tensor_copy(a[:, 4, :], mem.src[:, sl]))
                    step(v.scalar_tensor_tensor(out=mem.zrow[:, sl], in0=a[:, 4, :], scalar=float(K3), in1=k,
                                                op0=ALU.mult, op1=ALU.add))
                    for i2 in range(2):
                        for i1 in range(2):
                            step(v.tensor_tensor(a[:, 5, :], a[:, 11 + i2 + 6, :], a[:, 11 + i1 + 3, :], ALU.mult))
                            for i0 in range(2):
                                last = v.tensor_tensor(mem.chunk_basis[:, :, 4 * i2 + 2 * i1 + i0], a[:, 5, :],
                                                       a[:, 11 + i0, :], ALU.mult)
                                if (i2, i1, i0) != (1, 1, 1):
                                    step(last)
                    last.then_inc(s["tmp_free"], 1)
                    dve.wait_ge(s["tmp_free"], c + 1)


def store_table(nc, ctx, mem, phase, source, target):
    with semaphores(nc, phase, "stored") as s:
        with nc.Block() as block:
            @block.sync
            def _(sp):
                sp.dma_start(target, source).then_inc(s["stored"], 16)
                sp.wait_ge(s["stored"], 16)


def gather(nc, pool, mem, s, slot, g, sources):
    pool.wait_ge(s["index_ready"], g + 1)
    pool.wait_ge(s["stage_free"], g + 1)
    pool.sem_inc(s["pool_passed"], 1)
    for n, (table, width) in enumerate(sources):
        for j in range(J):
            nc.gpsimd.indirect_dma_start(
                mem.stage[:, slot, j, n * C:n * C + width], None, table,
                bass.IndirectOffsetOnAxis(mem.index[:, slot, n, j:j + 1], 0)).then_inc(s[f"gathered{slot}"], 16)


def copy_index(nc, mem, s, slot, g, indices):
    for n, index in enumerate(indices):
        last = nc.vector.tensor_copy(mem.index[:, slot, n, :], index[:, bass.ds(g * J, J)])
    last.then_inc(s["index_ready"], 1)


def message(nc, dve, mem, s, kind, slot, i, g, indices):
    v = nc.vector
    out = mem.msg[:, slot, :, :]
    if kind == "count":
        return
    rows = mem.stage[:, slot, :, :]
    weight = bcast(mem.weight[:, bass.ds(g * J, J)], C)
    arrived = 16 * J * (2 if kind == "laplacian" else 1)
    if kind == "spline":
        dve.wait_ge(s[f"spline{slot}"], 16 * (i + 1))
    dve.wait_ge(s[f"gathered{slot}"], arrived * (i + 1))
    if kind == "weighted":
        v.tensor_tensor(out, rows[:, :, 0:C], weight, ALU.mult).then_inc(s["stage_free"], 1)
    elif kind == "plain":
        v.tensor_copy(out, rows[:, :, 0:C]).then_inc(s["stage_free"], 1)
    elif kind == "laplacian":
        v.tensor_tensor(out, rows[:, :, 0:C], rows[:, :, C:2 * C], ALU.subtract).then_inc(s["stage_free"], 1)
        dve.wait_ge(s["stage_free"], g + 3)
        v.tensor_tensor(out, out, weight, ALU.mult).then_inc(s["part_done"], 1)
        dve.wait_ge(s["part_done"], g + 1)
    elif kind == "spline":
        w = mem.spline[:, slot, :].rearrange("p (j k) -> p j k", k=8)
        for i2 in range(2):
            for i1 in range(2):
                at = (i2 * KS * KS + i1 * KS) * C
                k = 4 * i2 + 2 * i1
                for i0 in range(2):
                    last = v.tensor_tensor(mem.prod[:, :, k + i0, :], rows[:, :, at + i0 * C:at + i0 * C + C],
                                           bcast(w[:, :, k + i0], C), ALU.mult)
        last.then_inc(s["stage_free"], 1)
        dve.wait_ge(s["stage_free"], g + 3)
        for n, half in enumerate((4, 2)):
            v.tensor_tensor(mem.prod[:, :, 0:half, :], mem.prod[:, :, 0:half, :],
                            mem.prod[:, :, half:2 * half, :], ALU.add).then_inc(s["part_done"], 1)
            dve.wait_ge(s["part_done"], 2 * g + n + 1)
        v.tensor_tensor(out, mem.prod[:, :, 0, :], mem.prod[:, :, 1, :], ALU.add).then_inc(s["sum_done"], 1)
        dve.wait_ge(s["sum_done"], g + 1)
    copy_index(nc, mem, s, slot, g + 2, indices)


SOURCES = {"count": 0, "weighted": 1, "plain": 1, "laplacian": 2, "spline": 1}
PROPAGATE = ("index_ready stage_free pool_passed spline0 spline1 part_done sum_done msg_ready "
             "scattered added wide_ready wide_free lhs_ready small_done dve_passed took_branch")


def propagate_window(nc, mem, s, kind, sources, indices):
    gathers = SOURCES[kind] > 0

    with nc.Block() as block:
        idle = "scalar" + ("" if gathers else " gpsimd") + ("" if kind == "spline" else " sync")
        pass_through(block, idle, s["took_branch"])

        if gathers:
            @block.gpsimd
            def _(pool):
                with pool.Fori(0, GROUPS // 2) as i:
                    for slot in range(2):
                        gather(nc, pool, mem, s, slot, 2 * i + slot, sources)

        if kind == "spline":
            @block.sync
            def _(sp):
                with sp.Fori(0, GROUPS // 2) as i:
                    for slot in range(2):
                        sp.wait_ge(s["stage_free"], 2 * i + slot + 1)
                        sp.dma_start(mem.spline[:, slot, :],
                                     mem.basis[:, bass.ds((2 * i + slot) * (J * 8), J * 8)]).then_inc(s[f"spline{slot}"], 16)

        @block.tensor
        def _(pe):
            with pe.Fori(0, GROUPS // 2) as i:
                for slot in range(2):
                    g = 2 * i + slot
                    pe.wait_ge(s["msg_ready"], g + 1)
                    pe.wait_ge(s["added"], g + 1)
                    for j in range(J):
                        last = nc.tensor.matmul(mem.ps[0:C, slot, 0:WINDOW], mem.msg[:, slot, j, :],
                                                mem.onehot[:, slot, j, :], start=(j == 0), stop=(j == J - 1))
                    last.then_inc(s["scattered"], 1)

        @block.vector
        def _(dve):
            v = nc.vector

            def prepare(i, slot, g):
                message(nc, dve, mem, s, kind, slot, i, g, indices)
                v.tensor_tensor(mem.onehot[:, slot, :, :],
                                bcast(mem.rel[:, bass.ds(g * J, J)], WINDOW),
                                mem.iota_win[:, :].unsqueeze(1).to_broadcast([P, J, WINDOW]),
                                ALU.is_equal).then_inc(s["msg_ready"], 1)

            def add(slot, g):
                base = dve.value_load(mem.base[0:1, bass.ds(g, 1)], min_val=0, max_val=NPAD)
                window = mem.acc[0:C, bass.ds(base, WINDOW)]
                dve.wait_ge(s["added"], g + 2)
                dve.sem_inc(s["dve_passed"], 1)
                dve.wait_ge(s["scattered"], g + 1)
                v.tensor_tensor(window, window, mem.ps[0:C, slot, 0:WINDOW], ALU.add).then_inc(s["added"], 1)

            dve.sem_inc(s["stage_free"], 2)
            dve.sem_inc(s["added"], 1)
            if gathers:
                copy_index(nc, mem, s, 0, 0, indices)
                copy_index(nc, mem, s, 1, 1, indices)
            else:
                v.memset(mem.msg[:, :, :, :], 1.0)
            v.memset(mem.acc[0:C, :], 0.0).then_inc(s["added"], 1)
            prepare(0, 0, 0)
            with dve.Fori(0, GROUPS // 2 - 1) as i:
                prepare(i, 1, 2 * i + 1)
                add(0, 2 * i)
                prepare(i + 1, 0, 2 * i + 2)
                add(1, 2 * i + 1)
            prepare(GROUPS // 2 - 1, 1, GROUPS - 1)
            add(0, GROUPS - 2)
            add(1, GROUPS - 1)


def propagate_all(nc, mem, s, kind, sources, indices, target):
    gathers = SOURCES[kind] > 0

    with nc.Block() as block:
        idle = "scalar" + ("" if gathers else " gpsimd") + ("" if kind == "spline" else " sync")
        pass_through(block, idle, s["took_branch"])

        if gathers:
            @block.gpsimd
            def _(pool):
                with pool.Fori(0, GROUPS // 2) as i:
                    for slot in range(2):
                        gather(nc, pool, mem, s, slot, 2 * i + slot, sources)

        if kind == "spline":
            @block.sync
            def _(sp):
                with sp.Fori(0, GROUPS // 2) as i:
                    for slot in range(2):
                        sp.wait_ge(s["stage_free"], 2 * i + slot + 1)
                        sp.dma_start(mem.spline[:, slot, :],
                                     mem.basis[:, bass.ds((2 * i + slot) * (J * 8), J * 8)]).then_inc(s[f"spline{slot}"], 16)

        @block.tensor
        def _(pe):
            for b in range(QBANKS):
                nc.tensor.matmul(mem.ps[:, b, 0:QCOLS], mem.zeros[:, 0:P], mem.zeros[:, 0:QCOLS], start=True,
                                 stop=False, skip_group_check=True)
            with pe.Fori(0, GROUPS // 2) as i:
                for slot in range(2):
                    g = 2 * i + slot
                    pe.wait_ge(s["lhs_ready"], g + 1)
                    for j in range(J):
                        pe.wait_ge(s["wide_ready"], g * J + j + 1)
                        for part in range(3):
                            for b in range(QBANKS):
                                last = nc.tensor.matmul(
                                    mem.ps[:, b, 0:QCOLS],
                                    mem.lhs[:, slot, j, part, :, :].rearrange("p q c -> p (q c)"),
                                    mem.wide[:, j % RING, b * QCOLS:(b + 1) * QCOLS],
                                    start=False, stop=False, skip_group_check=True)
                        last.then_inc(s["wide_free"], 1)

        @block.vector
        def _(dve):
            v = nc.vector

            def prepare(i, slot, g):
                message(nc, dve, mem, s, kind, slot, i, g, indices)
                chain = [0]

                def step(ins):
                    chain[0] += 1
                    ins.then_inc(s["small_done"], 1)
                    dve.wait_ge(s["small_done"], g * STEPS + chain[0])

                tgt = target[:, bass.ds(g * J, J)]
                step(v.tensor_single_scalar(mem.qpos_i[:, 0, :], tgt, Q - 1, ALU.bitwise_and))
                step(v.tensor_single_scalar(mem.qpos_i[:, 1, :], tgt, 2, ALU.arith_shift_right))
                step(v.tensor_copy(mem.qpos[:, slot, :, :], mem.qpos_i[:, :, :]))
                step(v.tensor_tensor(mem.qmask[:, :, :], bcast(mem.qpos[:, slot, 0, :], Q),
                                     mem.iota_win[:, 0:Q].unsqueeze(1).to_broadcast([P, J, Q]), ALU.is_equal))
                msg, first, second, third = mem.msg[:, slot, :, :], *(mem.part[:, n, :, :] for n in range(3))
                step(v.tensor_copy(first, msg))
                step(v.tensor_tensor(mem.rest[:, 0, :, :], msg, first, ALU.subtract))
                step(v.tensor_copy(second, mem.rest[:, 0, :, :]))
                step(v.tensor_tensor(mem.rest[:, 1, :, :], mem.rest[:, 0, :, :], second, ALU.subtract))
                step(v.tensor_copy(third, mem.rest[:, 1, :, :]))
                dve.wait_ge(s["wide_free"], (g + 1) * J)
                for n in range(3):
                    for q in range(Q):
                        last = v.tensor_tensor(mem.lhs[:, slot, :, n, q, :], mem.part[:, n, :, :],
                                               bcast(mem.qmask[:, :, q], C), ALU.mult)
                last.then_inc(s["lhs_ready"], 1)
                for j in range(J):
                    dve.wait_ge(s["wide_free"], g * J + j + 1 + 2 * J - RING)
                    v.tensor_scalar(mem.wide[:, j % RING, :], mem.iota_pos[:, :], mem.qpos[:, slot, 1, j:j + 1],
                                    None, ALU.is_equal).then_inc(s["wide_ready"], 1)

            STEPS = 9
            dve.sem_inc(s["stage_free"], 2)
            dve.sem_inc(s["wide_free"], 2 * J)
            if gathers:
                copy_index(nc, mem, s, 0, 0, indices)
                copy_index(nc, mem, s, 1, 1, indices)
            else:
                v.memset(mem.msg[:, :, :, :], 1.0)
            with dve.Fori(0, GROUPS // 2) as i:
                for slot in range(2):
                    prepare(i, slot, 2 * i + slot)
            dve.wait_ge(s["wide_free"], GROUPS * J + 2 * J)
            for b in range(QBANKS):
                v.tensor_copy(mem.acc[:, b * QCOLS:(b + 1) * QCOLS], mem.ps[:, b, 0:QCOLS])


def to_node_major(nc, mem, s, every):
    with nc.Block() as block:
        pass_through(block, "sync scalar gpsimd vector", s["took_branch"])

        @block.tensor
        def _(pe):
            if every:
                for m in range(M // Q):
                    b, col = divmod(m * Q * C, BANK)
                    nc.tensor.matmul(mem.ps[0:NP, 4 + b, col:col + Q * C],
                                     mem.acc[:, m:m + (NP - 1) * (M // Q) + 1:M // Q],
                                     mem.ident[:, :], start=True, stop=True)
            else:
                for m in range(M):
                    b, col = divmod(m * C, BANK)
                    nc.tensor.matmul(mem.ps[0:NP, 4 + b, col:col + C],
                                     mem.acc[0:C, m:m + (NP - 1) * M + 1:M],
                                     mem.ident[0:C, 0:C], start=True, stop=True)


def propagate(nc, ctx, mem, phase, kind, sources, indices, unsorted):
    with semaphores(nc, phase, PROPAGATE) as s:
        if sources:
            for slot in range(2):
                s[f"gathered{slot}"] = ctx.enter_context(nc.semaphore(f"{phase}_gathered{slot}"))
        if unsorted is None:
            propagate_all(nc, mem, s, kind, sources, indices, mem.src)
            to_node_major(nc, mem, s, True)
            return
        with nc.If(unsorted == 0):
            propagate_window(nc, mem, s, kind, sources, indices)
            to_node_major(nc, mem, s, False)
        with nc.Else():
            propagate_all(nc, mem, s, kind, sources, indices, mem.dst)
            to_node_major(nc, mem, s, True)


def nm3(ap):
    return ap[:, :].rearrange("p (m c) -> p m c", c=C)


def sums_nm(mem):
    return mem.ps[0:NP, 4:8, :].rearrange("p b (m c) -> p (b m) c", c=C)


def layernorm(v, act_sqrt, step, mem, value, out):
    mean, var, inv = (mem.stat[:, i, :] for i in range(3))
    step(v.tensor_reduce(mean, nm3(value), AX.X, ALU.add))
    step(v.tensor_scalar(mean, mean, 1.0 / C, None, ALU.mult))
    step(v.tensor_tensor(nm3(value), nm3(value), bcast(mean, C), ALU.subtract))
    step(v.tensor_tensor(mem.t[:, :], value[:, :], value[:, :], ALU.mult))
    step(v.tensor_reduce(var, nm3(mem.t), AX.X, ALU.add))
    step(v.tensor_scalar(var, var, 1.0 / C, EPS, ALU.mult, ALU.add))
    act_sqrt(var)
    step(v.reciprocal(inv, var))
    step(v.tensor_tensor(nm3(out), nm3(value), bcast(inv, C), ALU.mult))


def finish_propagation(nc, ctx, mem, phase, what, out=None, params=None):
    with semaphores(nc, phase, "chain sqrt_in sqrt_out value stored params col col_sum") as s:
        y = {"table": mem.y}.get(what, mem.x)

        with nc.Block() as block:
            @block.sync
            def _(sp):
                if params:
                    for n, ap in enumerate(params):
                        sp.dma_start(mem.vec[:, n, :], ap.unsqueeze(0).to_broadcast([NP, C])).then_inc(s["params"], 16)
                if out is not None:
                    sp.wait_ge(s["value"], 1)
                    if out.shape[0] == NPAD:
                        sp.dma_start(out.rearrange("(p m) c -> p (m c)", m=M), y[:, :]).then_inc(s["stored"], 16)
                        sp.wait_ge(s["stored"], 16)
                    else:
                        whole = NODES // M
                        sp.dma_start(out[0:whole * M, :].rearrange("(p m) c -> p (m c)", m=M),
                                     y[0:whole, :]).then_inc(s["stored"], 16)
                        sp.dma_start(out[whole * M:NODES, :].rearrange("(p m) c -> p (m c)", p=1),
                                     y[whole:whole + 1, 0:(NODES - whole * M) * C]).then_inc(s["stored"], 16)
                        sp.wait_ge(s["stored"], 32)

            @block.scalar
            def _(act):
                if what != "table" and what != "count":
                    act.wait_ge(s["sqrt_in"], 1)
                    if what.startswith("conv"):
                        ap = mem.vec[:, 5, :]
                    else:
                        ap = mem.stat[:, 1, :]
                    nc.scalar.activation(ap, ap, ACT.Sqrt).then_inc(s["sqrt_out"], 1)

            @block.tensor
            def _(pe):
                if what.startswith("conv"):
                    for n in range(2):
                        pe.wait_ge(s["col"], n + 1)
                        nc.tensor.matmul(mem.ps[0:NP, n, 0:C], mem.ones[0:NP, 0:NP], mem.vec[:, 3 + n, :],
                                         start=True, stop=True).then_inc(s["col_sum"], 1)

            @block.vector
            def _(dve):
                v = nc.vector
                step = Chain(dve, s["chain"])

                def act_sqrt(_):
                    dve.sem_inc(s["sqrt_in"], 1)
                    dve.wait_ge(s["sqrt_out"], 1)

                if what == "table":
                    v.tensor_copy(nm3(mem.y), sums_nm(mem)).then_inc(s["value"], 1)
                elif what == "count":
                    step(v.tensor_scalar(mem.inv_count[:, :], sums_nm(mem)[:, :, 0], 1.0, None, ALU.max))
                    step(v.reciprocal(mem.inv_count[:, :], mem.inv_count[:, :]))
                elif what == "residual":
                    step(v.tensor_tensor(nm3(mem.y), nm3(mem.x), sums_nm(mem), ALU.add))
                    layernorm(v, act_sqrt, step, mem, mem.y, mem.x)
                    dve.sem_inc(s["value"], 1)
                elif what in ("conv", "conv_last"):
                    dve.wait_ge(s["params"], 48)
                    mid = lambda n: mem.vec[:, n, :].unsqueeze(1).to_broadcast([NP, M, C])
                    step(v.tensor_tensor(nm3(mem.t), sums_nm(mem), bcast(mem.inv_count[:, :], C), ALU.mult))
                    step(v.tensor_tensor(mem.t[:, :], mem.t[:, :], mem.h[:, :], ALU.add))
                    step(v.tensor_tensor(nm3(mem.t), nm3(mem.t), mid(0), ALU.add))
                    if what == "conv":
                        step(v.scalar_tensor_tensor(out=mem.t[:, :], in0=mem.t[:, :], scalar=NEG, in1=mem.t[:, :],
                                                    op0=ALU.mult, op1=ALU.max))
                    step(v.tensor_tensor(mem.t[:, :], mem.t[:, :], mem.y[:, :], ALU.add))
                    by_feature = mem.h[:, :].rearrange("p (m c) -> p c m", c=C)
                    real = bcast(mem.mask[:, :], C)
                    step(v.tensor_tensor(nm3(mem.h), nm3(mem.t), real, ALU.mult))
                    v.tensor_reduce(mem.vec[:, 3, :], by_feature, AX.X, ALU.add).then_inc(s["col"], 1)
                    dve.wait_ge(s["col_sum"], 1)
                    step(v.tensor_scalar(mem.vec[:, 5, :], mem.ps[0:NP, 0, 0:C], 1.0 / NODES, None, ALU.mult))
                    step(v.tensor_tensor(nm3(mem.t), nm3(mem.t), mid(5), ALU.subtract))
                    step(v.tensor_tensor(nm3(mem.h), nm3(mem.t), real, ALU.mult))
                    step(v.tensor_tensor(mem.h[:, :], mem.h[:, :], mem.h[:, :], ALU.mult))
                    v.tensor_reduce(mem.vec[:, 4, :], by_feature, AX.X, ALU.add).then_inc(s["col"], 1)
                    dve.wait_ge(s["col_sum"], 2)
                    step(v.tensor_scalar(mem.vec[:, 5, :], mem.ps[0:NP, 1, 0:C], 1.0 / NODES, EPS, ALU.mult, ALU.add))
                    act_sqrt(None)
                    step(v.reciprocal(mem.vec[:, 5, :], mem.vec[:, 5, :]))
                    step(v.tensor_tensor(mem.vec[:, 5, :], mem.vec[:, 5, :], mem.vec[:, 1, :], ALU.mult))
                    step(v.tensor_tensor(nm3(mem.t), nm3(mem.t), mid(5), ALU.mult))
                    step(v.tensor_tensor(nm3(mem.y), nm3(mem.t), mid(2), ALU.add))


def residual_layernorm(nc, ctx, mem, phase, out):
    with semaphores(nc, phase, "chain sqrt_in sqrt_out value stored") as s:
        with nc.Block() as block:
            @block.sync
            def _(sp):
                sp.wait_ge(s["value"], 1)
                sp.dma_start(out.rearrange("(p m) c -> p (m c)", m=M), mem.x[:, :]).then_inc(s["stored"], 16)
                sp.wait_ge(s["stored"], 16)

            @block.scalar
            def _(act):
                act.wait_ge(s["sqrt_in"], 1)
                nc.scalar.activation(mem.stat[:, 1, :], mem.stat[:, 1, :], ACT.Sqrt).then_inc(s["sqrt_out"], 1)

            @block.vector
            def _(dve):
                v = nc.vector
                step = Chain(dve, s["chain"])

                def act_sqrt(_):
                    dve.sem_inc(s["sqrt_in"], 1)
                    dve.wait_ge(s["sqrt_out"], 1)

                step(v.tensor_tensor(mem.y[:, :], mem.x[:, :], mem.y[:, :], ALU.add))
                layernorm(v, act_sqrt, step, mem, mem.y, mem.x)
                dve.sem_inc(s["value"], 1)


def spline_table(nc, ctx, mem, phase, weights, root):
    with semaphores(nc, phase, "weights column_ready transposed xt_ready z_low z_high z_free_v z_free_s "
                                   "rows_v rows_s rows_free root_done stored0 stored1") as s:

        with nc.Block() as block:
            @block.sync
            def _(sp):
                sp.dma_start(mem.kernel_matrix, weights).then_inc(s["weights"], 16)
                sp.dma_start(mem.root[:, :], root).then_inc(s["weights"], 16)
                rows = mem.z.rearrange("(p m k) c -> p m (k c)", m=M, k=K3)

                def send(slot, m):
                    sp.wait_ge(s["rows_v"], m + 1)
                    sp.wait_ge(s["rows_s"], m + 1)
                    sp.dma_start(rows[:, bass.ds(m, 1), :].rearrange("p a f -> p (a f)"),
                                 mem.zout[:, slot, :]).then_inc(s[f"stored{slot}"], 16)

                def retire(slot, n):
                    sp.wait_ge(s[f"stored{slot}"], 16 * n)
                    sp.sem_inc(s["rows_free"], 1)

                send(0, 0)
                with sp.Fori(0, M // 2 - 1) as i:
                    send(1, 2 * i + 1)
                    retire(0, i + 1)
                    send(0, 2 * i + 2)
                    retire(1, i + 1)
                send(1, M - 1)
                retire(0, M // 2)
                retire(1, M // 2)

            @block.tensor
            def _(pe):
                pe.wait_ge(s["weights"], 32)
                with pe.Fori(0, M // 2) as i:
                    for slot in range(2):
                        m = 2 * i + slot
                        pe.wait_ge(s["column_ready"], m + 1)
                        nc.tensor.matmul(mem.ps[0:C, 4 + slot, 0:NP], mem.xslot[:, slot, :],
                                         mem.ident[0:NP, 0:NP], start=True, stop=True).then_inc(s["transposed"], 1)
                        pe.wait_ge(s["xt_ready"], m + 1)
                        nc.tensor.matmul(mem.ps[0:NP, 6 + slot, 0:C], mem.xtslot[:, slot, :],
                                         mem.root[:, :], start=True, stop=True).then_inc(s["root_done"], 1)
                        for half, (free, done) in enumerate((("z_free_v", "z_low"), ("z_free_s", "z_high"))):
                            pe.wait_ge(s[free], m + 1)
                            for b in (2 * half, 2 * half + 1):
                                last = nc.tensor.matmul(mem.ps[0:NP, b, :], mem.xtslot[:, slot, :],
                                                        mem.kernel_matrix[:, b * BANK:(b + 1) * BANK],
                                                        start=True, stop=True)
                            last.then_inc(s[done], 1)

            @block.scalar
            def _(act):
                act.sem_inc(s["z_free_s"], 1)
                with act.Fori(0, M // 2) as i:
                    for slot in range(2):
                        m = 2 * i + slot
                        act.wait_ge(s["rows_free"], m + 1)
                        act.wait_ge(s["z_high"], m + 1)
                        nc.scalar.activation(mem.zout[:, slot, 2 * BANK:4 * BANK].rearrange("p (b f) -> p b f", b=2),
                                             mem.ps[0:NP, 2:4, :], ACT.Copy).then_inc(s["rows_s"], 1)
                        act.wait_ge(s["rows_s"], m + 1)
                        act.sem_inc(s["z_free_s"], 1)

            @block.vector
            def _(dve):
                v = nc.vector
                dve.sem_inc(s["z_free_v"], 1)
                dve.sem_inc(s["rows_free"], 2)
                with dve.Fori(0, M // 2) as i:
                    for slot in range(2):
                        m = 2 * i + slot
                        v.tensor_copy(mem.xslot[:, slot, :], mem.y[:, bass.ds(m * C, C)]).then_inc(s["column_ready"], 1)
                        dve.wait_ge(s["transposed"], m + 1)
                        v.tensor_copy(mem.xtslot[:, slot, :], mem.ps[0:C, 4 + slot, 0:NP]).then_inc(s["xt_ready"], 1)
                        dve.wait_ge(s["root_done"], m + 1)
                        v.tensor_scalar(mem.h[:, bass.ds(m * C, C)], mem.ps[0:NP, 6 + slot, 0:C], 1.0, None, ALU.mult)
                        dve.wait_ge(s["rows_free"], m + 1)
                        dve.wait_ge(s["z_low"], m + 1)
                        v.tensor_copy(mem.zout[:, slot, 0:2 * BANK].rearrange("p (b f) -> p b f", b=2),
                                      mem.ps[0:NP, 0:2, :]).then_inc(s["rows_v"], 1)
                        dve.wait_ge(s["rows_v"], m + 1)
                        dve.sem_inc(s["z_free_v"], 1)


def build(nc, inp, out, force_all=False):
    with ExitStack() as ctx:
        mem = Memory(nc, ctx)
        table = [(mem.table, C)]
        setup(nc, ctx, mem, inp)
        unsorted = nc.values_load(mem.flag[0:1, 0:1], min_val=0, max_val=1)
        if force_all:
            unsorted = 1 - unsorted

        propagate(nc, ctx, mem, "count", "count", [], [], unsorted)
        finish_propagation(nc, ctx, mem, "count_end", "count")

        first = [(inp["x"], C)]
        for n in range(3):
            propagate(nc, ctx, mem, f"hop{n}", "weighted", table if n else first, [mem.dst], None)
            if n < 2:
                finish_propagation(nc, ctx, mem, f"hop{n}_end", "table", mem.table)
        finish_propagation(nc, ctx, mem, "hop2_end", "residual")

        keep_input(nc, ctx, mem)
        for n in range(3):
            w = [inp[f"L1_gnn_{name}{n + 1}"] for name in ("W", "R", "b", "g", "be")]
            spline_table(nc, ctx, mem, f"z{n}", w[0], w[1])
            propagate(nc, ctx, mem, f"conv{n}", "spline", [(mem.z, ROW)], [mem.zrow], unsorted)
            finish_propagation(nc, ctx, mem, f"conv{n}_end", "conv" if n < 2 else "conv_last", params=w[2:])
        residual_layernorm(nc, ctx, mem, "conv_residual", mem.table)

        propagate(nc, ctx, mem, "laplace", "laplacian", table + table, [mem.dst, mem.src], None)
        finish_propagation(nc, ctx, mem, "laplace_end", "residual", mem.table)
        propagate(nc, ctx, mem, "sum", "plain", table, [mem.dst], None)
        finish_propagation(nc, ctx, mem, "sum_end", "residual", out)


def keep_input(nc, ctx, mem):
    with semaphores(nc, "keep", "copied") as s:
        with nc.Block() as block:
            @block.vector
            def _(dve):
                nc.vector.tensor_copy(mem.y[:, :], mem.x[:, :]).then_inc(s["copied"], 1)
                dve.wait_ge(s["copied"], 1)


def kernel(**inputs):
    import numpy as np
    import concourse.bacc as bacc
    from concourse.bass_utils import run_bass_kernel_spmd

    arrays = {"x": np.zeros((NPAD, C), np.float32)}
    arrays["x"][:NODES] = np.asarray(inputs["x"])
    for name, fill in (("src", NODES), ("dst", NODES), ("edge_weight", 0), ("edge_attr_3", 0)):
        a = np.asarray(inputs[name])
        whole = np.full((TPAD * P,) + a.shape[1:], fill, a.dtype)
        whole[:EDGES] = a
        whole = np.moveaxis(whole.reshape((TPAD, P) + a.shape[1:]), 1, 0)
        if a.ndim == 2:
            whole = np.moveaxis(whole, 2, 1)
        if a.dtype.kind == "f":
            whole = whole[..., :TILES]
        arrays[name] = np.ascontiguousarray(whole)
    for n in (1, 2, 3):
        w = np.asarray(inputs[f"L1_gnn_W{n}"])
        arrays[f"L1_gnn_W{n}"] = np.ascontiguousarray(w.transpose(1, 0, 2).reshape(C, K3 * C))
        for name in ("R", "b", "g", "be"):
            arrays[f"L1_gnn_{name}{n}"] = np.ascontiguousarray(inputs[f"L1_gnn_{name}{n}"])

    nc = bacc.Bacc("TRN2", target_bir_lowering=False, num_devices=1)
    inp = {name: nc.dram_tensor(f"in_{name}", a.shape, mybir.dt.from_np(a.dtype), kind="ExternalInput").ap()
           for name, a in arrays.items()}
    out = nc.dram_tensor("out", (NODES, C), F32, kind="ExternalOutput").ap()
    build(nc, inp, out)
    r = run_bass_kernel_spmd(nc, [{f"in_{name}": a for name, a in arrays.items()}], core_ids=[0])
    return r.results[0]["out"]
```
